# Optimizing a Trainium2 kernel written in Bass

```python
import numpy as np
import jax
import jax.numpy as jnp

def _softmax(x, axis=-1):
    return jax.nn.softmax(x, axis=axis)

def _gelu(x):
    return jax.nn.gelu(x, approximate=True)

def _silu(x):
    return jax.nn.silu(x)

def _sigmoid(x):
    return jax.nn.sigmoid(x)

def _layernorm(x, axis=-1, eps=1e-05):
    m = jnp.mean(x, axis=axis, keepdims=True)
    v = jnp.var(x, axis=axis, keepdims=True)
    return (x - m) / jnp.sqrt(v + eps)

def _scatter_add(tgt, idx, src, axis=0):
    return tgt.at[idx].add(src)

def _segment_sum(src, seg, n):
    return jax.ops.segment_sum(src, seg, n)
kernel_name = 'mk_gnn_preln_d1_gnn_r64_d9b134'

def setup_inputs(seed: int=0):
    np.random.seed(seed)
    _w = jnp.asarray

    def _rec_inputs():
        import jax
        import jax.numpy as jnp
        _gk = jax.random.key(seed)
        x = -0.0005207 + 1.001 * jax.random.normal(jax.random.fold_in(_gk, 1), (50000, 256), jnp.float32)
        src = jax.random.randint(jax.random.fold_in(_gk, 2), (12500,), 0, 50000, jnp.int32)
        dst = jax.random.randint(jax.random.fold_in(_gk, 3), (12500,), 0, 50000, jnp.int32)
        _o = jnp.argsort(dst, stable=True)
        src = src[_o]
        dst = dst[_o]
        edge_weight = jax.random.uniform(jax.random.fold_in(_gk, 12), (12500,), jnp.float32, 0.0, 0.999998)
        node_vec = jax.random.uniform(jax.random.fold_in(_gk, 13), (50000,), jnp.float32, 0.0, 0.999833)
        return (x, src, dst, edge_weight, node_vec)
    x, src, dst, edge_weight, node_vec = _rec_inputs()

    def _L0_gnn_setup():
        import jax, jax.numpy as jnp
        import numpy as np
        from jax import lax
        N, E, D = (128, 4096, 256)
        NH, FOUT = (4, 64)
        D_STATE, D_CONV, DT_RANK = (16, 4, 16)

        def _layer_norm(x, g, b, eps=1e-05):
            mu = jnp.mean(x, -1, keepdims=True)
            var = jnp.var(x, -1, keepdims=True)
            return (x - mu) * lax.rsqrt(var + eps) * g + b

        def _mamba(xs, in_proj_w, conv_w, conv_b, x_proj_w, dt_proj_w, dt_proj_b, A_log, D_param, out_proj_w):
            n = xs.shape[0]
            xz = xs @ in_proj_w.T
            xc, z = jnp.split(xz, 2, axis=-1)
            K = conv_w.shape[1]
            xp = jnp.pad(xc, ((K - 1, 0), (0, 0)))
            xc = sum((xp[k:k + n] * conv_w[:, k] for k in range(K))) + conv_b
            xc = jax.nn.silu(xc)
            dbc = xc @ x_proj_w.T
            dt = jax.nn.softplus(dbc[:, :DT_RANK] @ dt_proj_w.T + dt_proj_b)
            Bm = dbc[:, DT_RANK:DT_RANK + D_STATE]
            Cm = dbc[:, DT_RANK + D_STATE:]
            A = -jnp.exp(A_log)
            dA = jnp.exp(dt[:, :, None] * A)
            dBx = (dt * xc)[:, :, None] * Bm[:, None, :]

            def step(h, t):
                dA_t, dBx_t, C_t = t
                h = dA_t * h + dBx_t
                return (h, h @ C_t)
            _, y = lax.scan(step, jnp.zeros((xc.shape[1], D_STATE), xs.dtype), (dA, dBx, Cm))
            y = y + xc * D_param
            y = y * jax.nn.silu(z)
            return y @ out_proj_w.T

        def _forward(x, edge_index, deg_noise, gat_w, gat_a_src, gat_a_tgt, gat_b, ln_local_g, ln_local_b, ln_global_g, ln_global_b, ln2_g, ln2_b, in_proj_w, conv_w, conv_b, x_proj_w, dt_proj_w, dt_proj_b, A_log, D_param, out_proj_w, wl, wg, ff1_w, ff1_b, ff2_w, ff2_b):
            n = x.shape[0]
            src, tgt = (edge_index[0], edge_index[1])
            proj = (x @ gat_w.T).reshape(n, NH, FOUT)
            s_src = jnp.sum(proj * gat_a_src, -1)
            s_tgt = jnp.sum(proj * gat_a_tgt, -1)
            e = jax.nn.leaky_relu(s_src[src] + s_tgt[tgt], 0.2)
            exp_e = jnp.exp(e - jnp.max(e))
            denom = jax.ops.segment_sum(exp_e, tgt, num_segments=n)
            attn = exp_e / (denom[tgt] + 1e-16)
            agg = jax.ops.segment_sum(proj[src] * attn[:, :, None], tgt, num_segments=n)
            h_local = jax.nn.elu((agg + x.reshape(n, NH, FOUT)).reshape(n, NH * FOUT) + gat_b)
            h_local = _layer_norm(h_local, ln_local_g, ln_local_b)
            deg = jax.ops.segment_sum(jnp.ones((src.shape[0],), x.dtype), src, num_segments=n)
            perm = jnp.argsort(deg + deg_noise, stable=True)
            inv = jnp.argsort(perm)
            y = _mamba(x[perm], in_proj_w, conv_w, conv_b, x_proj_w, dt_proj_w, dt_proj_b, A_log, D_param, out_proj_w)
            h_attn = _layer_norm(x + y[inv], ln_global_g, ln_global_b)
            gate = jax.nn.sigmoid(h_local @ wl.T + h_attn @ wg.T)
            h = gate * h_local + (1.0 - gate) * h_attn
            ff = jax.nn.relu(h @ ff1_w.T + ff1_b) @ ff2_w.T + ff2_b
            return _layer_norm(h + ff, ln2_g, ln2_b)
        key = jax.random.key(seed)
        ks = jax.random.split(key, 24)
        w = lambda i, shape, s=0.05: jax.random.normal(ks[i], shape, dtype=jnp.float32) * s
        return {'x': jax.random.normal(ks[0], (N, D), dtype=jnp.float32), 'edge_index': jax.random.randint(ks[1], (2, E), 0, N, dtype=jnp.int32), 'edge_prob': jax.random.uniform(ks[2], (E,), dtype=jnp.float32), 'deg_noise': jax.random.uniform(ks[3], (N,), dtype=jnp.float32), 'gat_w': w(4, (NH * FOUT, D)), 'gat_a_src': w(5, (NH, FOUT)), 'gat_a_tgt': w(6, (NH, FOUT)), 'gat_b': jnp.zeros((NH * FOUT,), jnp.float32), 'ln_local_g': jnp.ones((D,), jnp.float32), 'ln_local_b': jnp.zeros((D,), jnp.float32), 'ln_global_g': jnp.ones((D,), jnp.float32), 'ln_global_b': jnp.zeros((D,), jnp.float32), 'ln2_g': jnp.ones((D,), jnp.float32), 'ln2_b': jnp.zeros((D,), jnp.float32), 'in_proj_w': w(7, (2 * D, D)), 'conv_w': w(8, (D, D_CONV), 0.2), 'conv_b': jnp.zeros((D,), jnp.float32), 'x_proj_w': w(9, (DT_RANK + 2 * D_STATE, D)), 'dt_proj_w': w(10, (D, DT_RANK)), 'dt_proj_b': w(11, (D,), 0.1) - 4.0, 'A_log': jnp.log(jnp.tile(jnp.arange(1, D_STATE + 1, dtype=jnp.float32), (D, 1))), 'D_param': jnp.ones((D,), jnp.float32), 'out_proj_w': w(12, (D, D)), 'wl': w(13, (D, D)), 'wg': w(14, (D, D)), 'ff1_w': w(15, (2 * D, D)), 'ff1_b': jnp.zeros((2 * D,), jnp.float32), 'ff2_w': w(16, (D, 2 * D)), 'ff2_b': jnp.zeros((D,), jnp.float32)}
    _L0_gnn_all = _L0_gnn_setup()
    _L0_gnn_in = {k: v for k, v in _L0_gnn_all.items() if k in ('gat_w', 'gat_a_src', 'gat_a_tgt', 'gat_b', 'ln_local_g', 'ln_local_b', 'ln_global_g', 'ln_global_b', 'ln2_g', 'ln2_b', 'in_proj_w', 'conv_w', 'conv_b', 'x_proj_w', 'dt_proj_w', 'dt_proj_b', 'A_log', 'D_param', 'out_proj_w', 'wl', 'wg', 'ff1_w', 'ff1_b', 'ff2_w', 'ff2_b')}
    del _L0_gnn_all
    return {'x': x, 'src': src, 'dst': dst, 'edge_weight': edge_weight, 'node_vec': node_vec, 'L0_gnn_gat_w': _L0_gnn_in['gat_w'], 'L0_gnn_gat_a_src': _L0_gnn_in['gat_a_src'], 'L0_gnn_gat_a_tgt': _L0_gnn_in['gat_a_tgt'], 'L0_gnn_gat_b': _L0_gnn_in['gat_b'], 'L0_gnn_ln_local_g': _L0_gnn_in['ln_local_g'], 'L0_gnn_ln_local_b': _L0_gnn_in['ln_local_b'], 'L0_gnn_ln_global_g': _L0_gnn_in['ln_global_g'], 'L0_gnn_ln_global_b': _L0_gnn_in['ln_global_b'], 'L0_gnn_ln2_g': _L0_gnn_in['ln2_g'], 'L0_gnn_ln2_b': _L0_gnn_in['ln2_b'], 'L0_gnn_in_proj_w': _L0_gnn_in['in_proj_w'], 'L0_gnn_conv_w': _L0_gnn_in['conv_w'], 'L0_gnn_conv_b': _L0_gnn_in['conv_b'], 'L0_gnn_x_proj_w': _L0_gnn_in['x_proj_w'], 'L0_gnn_dt_proj_w': _L0_gnn_in['dt_proj_w'], 'L0_gnn_dt_proj_b': _L0_gnn_in['dt_proj_b'], 'L0_gnn_A_log': _L0_gnn_in['A_log'], 'L0_gnn_D_param': _L0_gnn_in['D_param'], 'L0_gnn_out_proj_w': _L0_gnn_in['out_proj_w'], 'L0_gnn_wl': _L0_gnn_in['wl'], 'L0_gnn_wg': _L0_gnn_in['wg'], 'L0_gnn_ff1_w': _L0_gnn_in['ff1_w'], 'L0_gnn_ff1_b': _L0_gnn_in['ff1_b'], 'L0_gnn_ff2_w': _L0_gnn_in['ff2_w'], 'L0_gnn_ff2_b': _L0_gnn_in['ff2_b']}

def reference(x, src, dst, edge_weight, node_vec, L0_gnn_gat_w, L0_gnn_gat_a_src, L0_gnn_gat_a_tgt, L0_gnn_gat_b, L0_gnn_ln_local_g, L0_gnn_ln_local_b, L0_gnn_ln_global_g, L0_gnn_ln_global_b, L0_gnn_ln2_g, L0_gnn_ln2_b, L0_gnn_in_proj_w, L0_gnn_conv_w, L0_gnn_conv_b, L0_gnn_x_proj_w, L0_gnn_dt_proj_w, L0_gnn_dt_proj_b, L0_gnn_A_log, L0_gnn_D_param, L0_gnn_out_proj_w, L0_gnn_wl, L0_gnn_wg, L0_gnn_ff1_w, L0_gnn_ff1_b, L0_gnn_ff2_w, L0_gnn_ff2_b):
    import jax
    import jax.numpy as jnp

    def _L0_gnn_ref(x, edge_index, edge_prob, deg_noise, gat_w, gat_a_src, gat_a_tgt, gat_b, ln_local_g, ln_local_b, ln_global_g, ln_global_b, ln2_g, ln2_b, in_proj_w, conv_w, conv_b, x_proj_w, dt_proj_w, dt_proj_b, A_log, D_param, out_proj_w, wl, wg, ff1_w, ff1_b, ff2_w, ff2_b):
        import jax, jax.numpy as jnp
        import numpy as np
        from jax import lax
        N, E, D = (128, 4096, 256)
        NH, FOUT = (4, 64)
        D_STATE, D_CONV, DT_RANK = (16, 4, 16)

        def _layer_norm(x, g, b, eps=1e-05):
            mu = jnp.mean(x, -1, keepdims=True)
            var = jnp.var(x, -1, keepdims=True)
            return (x - mu) * lax.rsqrt(var + eps) * g + b

        def _mamba(xs, in_proj_w, conv_w, conv_b, x_proj_w, dt_proj_w, dt_proj_b, A_log, D_param, out_proj_w):
            n = xs.shape[0]
            xz = xs @ in_proj_w.T
            xc, z = jnp.split(xz, 2, axis=-1)
            K = conv_w.shape[1]
            xp = jnp.pad(xc, ((K - 1, 0), (0, 0)))
            xc = sum((xp[k:k + n] * conv_w[:, k] for k in range(K))) + conv_b
            xc = jax.nn.silu(xc)
            dbc = xc @ x_proj_w.T
            dt = jax.nn.softplus(dbc[:, :DT_RANK] @ dt_proj_w.T + dt_proj_b)
            Bm = dbc[:, DT_RANK:DT_RANK + D_STATE]
            Cm = dbc[:, DT_RANK + D_STATE:]
            A = -jnp.exp(A_log)
            dA = jnp.exp(dt[:, :, None] * A)
            dBx = (dt * xc)[:, :, None] * Bm[:, None, :]

            def step(h, t):
                dA_t, dBx_t, C_t = t
                h = dA_t * h + dBx_t
                return (h, h @ C_t)
            _, y = lax.scan(step, jnp.zeros((xc.shape[1], D_STATE), xs.dtype), (dA, dBx, Cm))
            y = y + xc * D_param
            y = y * jax.nn.silu(z)
            return y @ out_proj_w.T

        def _forward(x, edge_index, deg_noise, gat_w, gat_a_src, gat_a_tgt, gat_b, ln_local_g, ln_local_b, ln_global_g, ln_global_b, ln2_g, ln2_b, in_proj_w, conv_w, conv_b, x_proj_w, dt_proj_w, dt_proj_b, A_log, D_param, out_proj_w, wl, wg, ff1_w, ff1_b, ff2_w, ff2_b):
            n = x.shape[0]
            src, tgt = (edge_index[0], edge_index[1])
            proj = (x @ gat_w.T).reshape(n, NH, FOUT)
            s_src = jnp.sum(proj * gat_a_src, -1)
            s_tgt = jnp.sum(proj * gat_a_tgt, -1)
            e = jax.nn.leaky_relu(s_src[src] + s_tgt[tgt], 0.2)
            exp_e = jnp.exp(e - jnp.max(e))
            denom = jax.ops.segment_sum(exp_e, tgt, num_segments=n)
            attn = exp_e / (denom[tgt] + 1e-16)
            agg = jax.ops.segment_sum(proj[src] * attn[:, :, None], tgt, num_segments=n)
            h_local = jax.nn.elu((agg + x.reshape(n, NH, FOUT)).reshape(n, NH * FOUT) + gat_b)
            h_local = _layer_norm(h_local, ln_local_g, ln_local_b)
            deg = jax.ops.segment_sum(jnp.ones((src.shape[0],), x.dtype), src, num_segments=n)
            perm = jnp.argsort(deg + deg_noise, stable=True)
            inv = jnp.argsort(perm)
            y = _mamba(x[perm], in_proj_w, conv_w, conv_b, x_proj_w, dt_proj_w, dt_proj_b, A_log, D_param, out_proj_w)
            h_attn = _layer_norm(x + y[inv], ln_global_g, ln_global_b)
            gate = jax.nn.sigmoid(h_local @ wl.T + h_attn @ wg.T)
            h = gate * h_local + (1.0 - gate) * h_attn
            ff = jax.nn.relu(h @ ff1_w.T + ff1_b) @ ff2_w.T + ff2_b
            return _layer_norm(h + ff, ln2_g, ln2_b)
        return _forward(x, edge_index, deg_noise, gat_w, gat_a_src, gat_a_tgt, gat_b, ln_local_g, ln_local_b, ln_global_g, ln_global_b, ln2_g, ln2_b, in_proj_w, conv_w, conv_b, x_proj_w, dt_proj_w, dt_proj_b, A_log, D_param, out_proj_w, wl, wg, ff1_w, ff1_b, ff2_w, ff2_b)
    edge_index = jnp.stack([src, dst])
    h = jnp.maximum(_layernorm(x, axis=-1), 0.0)
    x = x + _L0_gnn_ref(h, edge_index, edge_weight, node_vec, L0_gnn_gat_w, L0_gnn_gat_a_src, L0_gnn_gat_a_tgt, L0_gnn_gat_b, L0_gnn_ln_local_g, L0_gnn_ln_local_b, L0_gnn_ln_global_g, L0_gnn_ln_global_b, L0_gnn_ln2_g, L0_gnn_ln2_b, L0_gnn_in_proj_w, L0_gnn_conv_w, L0_gnn_conv_b, L0_gnn_x_proj_w, L0_gnn_dt_proj_w, L0_gnn_dt_proj_b, L0_gnn_A_log, L0_gnn_D_param, L0_gnn_out_proj_w, L0_gnn_wl, L0_gnn_wg, L0_gnn_ff1_w, L0_gnn_ff1_b, L0_gnn_ff2_w, L0_gnn_ff2_b)
    return x

_drawn_inputs = setup_inputs


def setup_inputs(seed=0):
    import zlib

    import numpy as np

    out = dict(_drawn_inputs(seed))
    spreads = {'L0_gnn_gat_b': (0.0, 0.1),
     'L0_gnn_ln_local_g': (1.0, 0.2),
     'L0_gnn_ln_local_b': (0.0, 0.1),
     'L0_gnn_ln_global_g': (1.0, 0.2),
     'L0_gnn_ln_global_b': (0.0, 0.1),
     'L0_gnn_ln2_g': (1.0, 0.2),
     'L0_gnn_ln2_b': (0.0, 0.1),
     'L0_gnn_conv_b': (0.0, 0.8),
     'L0_gnn_D_param': (1.0, 0.6),
     'L0_gnn_ff1_b': (0.0, 0.1),
     'L0_gnn_ff2_b': (0.0, 0.1)}
    factors = {'node_vec': 5.083,
     'L0_gnn_gat_a_src': 36.052,
     'L0_gnn_gat_a_tgt': 64.0,
     'L0_gnn_in_proj_w': 3.351,
     'L0_gnn_conv_w': 3.369,
     'L0_gnn_x_proj_w': 8.0,
     'L0_gnn_dt_proj_w': 8.0,
     'L0_gnn_dt_proj_b': 8.0,
     'L0_gnn_A_log': 8.0,
     'L0_gnn_out_proj_w': 3.286}
    for name, (base, spread) in spreads.items():
        noise = np.random.default_rng([zlib.crc32(name.encode()), seed]).standard_normal(out[name].shape)
        drawn = base * np.exp(spread * noise) if base else spread * noise
        out[name] = jnp.asarray(drawn.astype(out[name].dtype))
    for name, factor in factors.items():
        out[name] = (out[name] * factor).astype(out[name].dtype)
    return out
```

```python
from contextlib import ExitStack

import concourse.bass as bass
from concourse import mybir

ALU = mybir.AluOpType
ACT = mybir.ActivationFunctionType
AX_X = mybir.AxisListType.X
F32 = mybir.dt.float32
BF16 = mybir.dt.bfloat16
I32 = mybir.dt.int32
RMAX = bass.bass_isa.ReduceOp.max

P = 128
D = 256
HALVES = D // P
NH, FOUT = 4, 64
AW = D + NH
NS = 16
RANK = 16
TAPS = 4
CH = 512
SUB = CH // P
PLACES = P * CH
FF = 2 * D
EPS = 1e-5
BIG = 3.4028234e38
FAR = -3.0e38
LN_MAX = 1e18
SMALL = 1 / 256
AHEAD = 3


class Steps:

    def __init__(self, sem, names):
        self.sem, self.names = sem, names.split()
        self.place = {name: i + 1 for i, name in enumerate(self.names)}

    def start(self, eng):
        eng.sem_inc(self.sem, AHEAD * len(self.names))

    def at(self, c, name):
        return (c + AHEAD) * len(self.names) + self.place[name]

    def wait(self, eng, c, name):
        eng.wait_ge(self.sem, self.at(c, name))

    def done(self, ins, name):
        assert name in self.place
        ins.then_inc(self.sem, 1)


def build(nc, a, out):
    N = a["x"].shape[0]
    E = a["src"].shape[0]
    NC = -(-N // CH)
    ET = -(-E // P)
    ET += ET % 2
    NPAD = -(-(N + P) // P) * P
    assert N < PLACES and NC >= 5 and (NC - 2) % 3 == 0

    agg = nc.dram_tensor("agg_table", (NPAD, AW), F32, kind="Internal").ap()

    with ExitStack() as ctx:
        ctx.enter_context(nc.allow_non_contiguous_dma(reason="vectors by channel, a few hundred words each"))

        def sb(name, shape, dt=F32, c=ctx):
            return c.enter_context(nc.sbuf_tensor(name, shape, dt))

        def sem(name):
            return ctx.enter_context(nc.semaphore(name))

        s_alone = sem("s_alone")

        def alone(eng):
            eng.sem_inc(s_alone, 1)

        ident = sb("ident", [P, P])
        eps_c = sb("eps_c", [P, 1])
        one_c = sb("one_c", [P, 1])
        mhalf_c = sb("mhalf_c", [P, 1])
        ones_row = sb("ones_row", [1, P])
        in_w = sb("in_w", [P, HALVES, 2 * D])
        xp_w = sb("xp_w", [P, HALVES, 2 * NS + RANK])
        dt_w = sb("dt_w", [2 * NS + RANK, D])
        out_w = sb("out_w", [P, HALVES, D])
        wl_w = sb("wl_w", [P, HALVES, D])
        wg_w = sb("wg_w", [P, HALVES, D])
        ff1_w = sb("ff1_w", [P, HALVES, FF])
        ff2_w = sb("ff2_w", [P, FF // P, D])
        cols = sb("cols", [P, 7, HALVES])
        LLG, LLB, LGG, LGB, DTB, DPR, CVB = range(7)
        conv_w = sb("conv_w", [P, HALVES, TAPS])
        a_neg = sb("a_neg", [P, HALVES, NS])
        ff1_b = sb("ff1_b", [P, FF // P])
        rows = sb("rows", [1, 4, D])
        row_bc = sb("row_bc", [P, 3, D])
        GATB, LN2G, LN2B, FF2B = range(4)
        sel = sb("sel", [3 * 2 * NS, 2 * NS, P], BF16)
        perm = sb("perm", [P, SUB, P], I32)

        p1 = ExitStack()
        with p1:
            def s1(name, shape, dt=F32):
                return sb(name, shape, dt, p1)

            gat_wT = s1("gat_wT", [P, HALVES, D])
            gat_wr = s1("gat_wr", [P, HALVES, D])
            a_blk = s1("a_blk", [P, HALVES, 2, NH])
            wa = s1("wa", [P, HALVES, 2, NH])
            src_i = s1("src_i", [P, ET], I32)
            dst_i = s1("dst_i", [P, ET], I32)
            part_i = s1("part_i", [P, ET], I32)
            eidx_hi = s1("eidx_hi", [P, ET], I32)
            eidx_lo = s1("eidx_lo", [P, ET], I32)
            src_hi = s1("src_hi", [P, ET])
            src_lo = s1("src_lo", [P, ET])
            dst_f = s1("dst_f", [P, ET])
            iota_row = s1("iota_row", [P, CH])
            dump_f = s1("dump_f", [P, 1])
            pad_m = s1("pad_m", [P, ET])
            low_tri = s1("low_tri", [P, P])
            zeros = s1("zeros", [P, 8 * AW])
            zeros_b = s1("zeros_b", [P, CH], BF16)
            ecur = s1("ecur", [P, 2, 2], I32)
            xe = s1("xe", [P, 2, 2, D])
            he = s1("he", [P, 2, 2, D])
            est = s1("est", [P, 4, 6])
            emv = s1("emv", [P, 4, 2])
            ers = s1("ers", [P, 4])
            enm = s1("enm", [P, 4])
            heT = s1("heT", [P, 2, 2, HALVES, P])
            oh_hi = s1("oh_hi", [P, 2, P], BF16)
            oh_lo = s1("oh_lo", [P, 2, CH], BF16)
            proj = s1("proj", [P, ET, AW])
            elog = s1("elog", [P, ET, NH])
            eexp = s1("eexp", [P, ET, NH])
            emax = s1("emax", [P, 4])
            dcb = s1("dcb", [P, 2, P])
            same = s1("same", [P, 2, P])
            junk = s1("junk", [P, 2, P])
            cnt = s1("cnt", [P, 2])
            gap = s1("gap", [P, 2])
            pick = s1("pick", [P, 2])
            eidx = s1("eidx", [P, 2], I32)
            ev = s1("ev", [P, 2, AW])
            esum = s1("esum", [P, 2, AW])
            KI = s1("KI", [P, 2, 2, CH])
            pl_i = s1("pl_i", [P, CH], I32)
            gray = s1("gray", [P, CH], I32)
            sgn_i = s1("sgn_i", [P, CH], I32)
            sgn = s1("sgn", [P, CH])
            cmp_ge = s1("cmp_ge", [P, 2, CH // 2])
            cmp_le = s1("cmp_le", [P, CH // 2])
            cmp_w = s1("cmp_w", [P, CH // 2])
            swap = s1("swap", [P, CH // 2], I32)

            ps_deg = p1.enter_context(nc.psum_tensor("ps_deg", [P, CH], F32))
            ps_T = [p1.enter_context(nc.psum_tensor(f"ps_T{i}", [P, CH], F32)) for i in range(2)]
            ps_M = [p1.enter_context(nc.psum_tensor(f"ps_M{i}", [P, CH], F32)) for i in range(2)]
            ps_S = [p1.enter_context(nc.psum_tensor(f"ps_S{i}", [P, CH], F32)) for i in range(2)]

            s_weights = sem("s_weights")
            s_edges = sem("s_edges")
            s_noise = sem("s_noise")
            s_table = sem("s_table")
            s_zero = sem("s_zero")
            s_const = sem("s_const")
            s_setup = sem("s_setup")
            s_prep_pe = sem("s_prep_pe")
            s_prep_act = sem("s_prep_act")
            s_rows = sem("s_rows")
            s_gath = sem("s_gath")
            s_scat = [sem(f"s_scat{i}") for i in range(2)]
            s_max = sem("s_max")
            s_hist = sem("s_hist")
            s_prep = sem("s_prep")
            s_sort = sem("s_sort")
            s_turn_pe = sem("s_turn_pe")
            s_turn_act = sem("s_turn_act")
            s_icopy = sem("s_icopy")
            ea_pool = Steps(sem("ea_pool"), "idx")
            ea_act = Steps(sem("ea_act"), "ln rstd relu0 relu1 hT0 hT1 proj0 proj1")
            ea_dve = Steps(sem("ea_dve"), "stats aggr nmr onehot0 onehot1")
            ea_pe = Steps(sem("ea_pe"), "T0 T1 mm0 mm1 hist0 hist1")
            eb_dve = Steps(sem("eb_dve"), "dcb same0 same1 cnt gap pick idx v")
            eb_pe = Steps(sem("eb_pe"), "dT0 dT1 sum0 sum1")
            eb_act = Steps(sem("eb_act"), "sum0 sum1")

            def whole(tile):
                return tile[tuple([slice(None)] * len(tile.shape))]

            def by_half(ap):
                return ap.rearrange("(k p) n -> p k n", p=P)

            weight_loads = [
                (gat_wT, by_half(a["gat_wT"])), (gat_wr, by_half(a["gat_w"])), (in_w, by_half(a["in_projT"])),
                (xp_w, by_half(a["x_projT"])), (out_w, by_half(a["out_projT"])), (wl_w, by_half(a["wlT"])),
                (wg_w, by_half(a["wgT"])), (ff1_w, by_half(a["ff1T"])), (ff2_w, by_half(a["ff2T"])),
                (conv_w, by_half(a["conv_w"])), (a_neg, by_half(a["A_log"])),
            ]
            col_loads = [(LLG, "ln_local_g"), (LLB, "ln_local_b"), (LGG, "ln_global_g"), (LGB, "ln_global_b"),
                         (DTB, "dt_proj_b"), (DPR, "D_param"), (CVB, "conv_b")]
            row_loads = [(GATB, "gat_b"), (LN2G, "ln2_g"), (LN2B, "ln2_b"), (FF2B, "ff2_b")]
            N_LOADS = len(weight_loads) + len(col_loads) + len(row_loads) + 2 + 2 * NH

            full_e, rest_e = E // ET, E % ET
            edge_dmas = 2 * (bool(full_e) + bool(rest_e))
            full_n, rest_n = N // CH, N % CH
            noise_dmas = bool(full_n) + bool(rest_n)
            table = agg.rearrange("(p r) w -> p (r w)", p=P)
            table_len = NPAD // P * AW
            zero_len = zeros.shape[1]
            table_dmas = -(-table_len // zero_len)

            (C_EPS, C_ONES, C_IOTA, C_DUMP, C_PART, C_SRC, C_DST, C_ZERO, C_ZB, C_ABLK, C_KEYS, C_INDEX,
             C_PL, C_MEM, C_ID, C_TRI, C_SEL0, C_SEL1, C_SEL) = range(1, 20)

            KEY_BITS, ROW_BITS = 16, 9
            plan, cur, dve_ops, stages, turns = [], 0, 0, 0, 0

            def add(kind, k, dist, ops):
                nonlocal cur, dve_ops, stages, turns
                plan.append(dict(kind=kind, k=k, dist=dist, cur=cur, begin=dve_ops, end=dve_ops + ops,
                                 stages=stages, turns=turns))
                dve_ops += ops
                if kind == "stage":
                    stages += 1
                if kind == "turn":
                    turns += 1
                if kind != "sign":
                    cur = 1 - cur

            for k in range(1, KEY_BITS + 1):
                add("sign", k, 0, 3)
                if k > ROW_BITS:
                    add("turn", k, 0, 1)
                    for j in range(k - 1, ROW_BITS - 1, -1):
                        add("stage", k, 1 << (j - ROW_BITS), 8)
                    add("turn", k, 0, 1)
                for j in range(min(k, ROW_BITS) - 1, -1, -1):
                    add("stage", k, 1 << j, 8)
            add("turn", KEY_BITS, 0, 0)
            last_turn = plan.pop()
            SORT0 = 3

            block = p1.enter_context(nc.Block())

            @block.sync
            def _(sp):
                sp.wait_ge(s_const, C_DST)
                for tile, name in ((src_i, "src"), (dst_i, "dst")):
                    if full_e:
                        sp.dma_start(tile[0:full_e, :], a[name][0:full_e * ET].rearrange("(p t) -> p t", t=ET))\
                          .then_inc(s_edges, 16)
                    if rest_e:
                        sp.dma_start(tile[full_e:full_e + 1, 0:rest_e],
                                     a[name][full_e * ET:E].rearrange("(p t) -> p t", p=1)).then_inc(s_edges, 16)
                sp.wait_ge(s_const, C_ABLK)
                for h in range(NH):
                    rows_h = slice(h * FOUT % P, h * FOUT % P + FOUT)
                    for j, name in enumerate(("gat_a_src", "gat_a_tgt")):
                        sp.dma_start(a_blk[rows_h, h * FOUT // P, j, h:h + 1],
                                     a[name][h, :].rearrange("(f o) -> f o", o=1)).then_inc(s_weights, 16)
                sp.wait_ge(s_const, C_KEYS)
                sp.dma_start(KI[0:full_n, 0, 0, :], a["noise"][0:full_n * CH].rearrange("(p t) -> p t", t=CH))\
                  .then_inc(s_noise, 16)
                if rest_n:
                    sp.dma_start(KI[full_n:full_n + 1, 0, 0, 0:rest_n],
                                 a["noise"][full_n * CH:N].rearrange("(p t) -> p t", p=1)).then_inc(s_noise, 16)
                for i in range(0, table_len, zero_len):
                    m = min(zero_len, table_len - i)
                    sp.dma_start(table[:, i:i + m], zeros[:, 0:m]).then_inc(s_table, 16)
                sp.wait_ge(s_table, 16 * table_dmas)

            @block.gpsimd
            def _(pool):
                ea_pool.start(pool)
                nc.gpsimd.memset(eps_c[:, :], EPS).then_inc(s_const, 1)
                nc.gpsimd.memset(ones_row[:, :], 1.0).then_inc(s_const, 1)
                nc.gpsimd.iota(iota_row[:, :], [[1, CH]], base=0, channel_multiplier=0,
                               allow_small_or_imprecise_dtypes=True).then_inc(s_const, 1)
                nc.gpsimd.iota(dump_f[:, :], [[1, 1]], base=N, channel_multiplier=1,
                               allow_small_or_imprecise_dtypes=True).then_inc(s_const, 1)
                nc.gpsimd.iota(part_i[:, :], [[1, ET]], base=0, channel_multiplier=ET).then_inc(s_const, 1)
                nc.gpsimd.memset(src_i[:, :], PLACES - 1).then_inc(s_const, 1)
                nc.gpsimd.memset(dst_i[:, :], N).then_inc(s_const, 1)
                nc.gpsimd.memset(zeros[:, :], 0.0).then_inc(s_const, 1)
                nc.gpsimd.memset(zeros_b[:, :], 0.0).then_inc(s_const, 1)
                nc.gpsimd.memset(a_blk[:, :, :, :], 0.0).then_inc(s_const, 1)
                nc.gpsimd.memset(KI[:, 0, 0, :], BIG).then_inc(s_const, 1)
                nc.gpsimd.iota(KI[:, 0, 1, :], [[1, CH]], base=0, channel_multiplier=CH,
                               allow_small_or_imprecise_dtypes=True).then_inc(s_const, 1)
                nc.gpsimd.iota(pl_i[:, :], [[1, CH]], base=0, channel_multiplier=CH).then_inc(s_const, 1)
                nc.gpsimd.memset(ident[:, :], 0.0)
                nc.gpsimd.memset(low_tri[:, :], 1.0)
                nc.gpsimd.memset(xe[:, :, :, :], 0.0)
                nc.gpsimd.memset(sel[:, :, :], 0.0).then_inc(s_const, 1)
                pool.wait_ge(s_const, C_MEM)
                nc.gpsimd.affine_select(out=ident[:, :], in_=ident[:, :], compare_op=ALU.not_equal, fill=1.0,
                                        base=0, pattern=[[-1, P]], channel_multiplier=1).then_inc(s_const, 1)
                nc.gpsimd.affine_select(out=low_tri[:, :], in_=low_tri[:, :], compare_op=ALU.is_gt, fill=0.0,
                                        base=0, pattern=[[-1, P]], channel_multiplier=1).then_inc(s_const, 1)
                for part in range(3):
                    pool.wait_ge(s_const, C_TRI + part)
                    nc.gpsimd.affine_select(out=sel[:, :, :], in_=sel[:, :, :], compare_op=ALU.not_equal, fill=1.0,
                                            base=-2 * NS * part, pattern=[[-1, 2 * NS], [0, P]],
                                            channel_multiplier=1).then_inc(s_const, 1)

                pool.wait_ge(s_edges, 16 * edge_dmas)
                with pool.Fori(0, ET // 2) as i:
                    ea_act.wait(pool, i - 1, "relu1")
                    ea_dve.wait(pool, i - 1, "stats")
                    nc.gpsimd.tensor_copy(ecur[:, :, 0], src_i[:, bass.ds(i * 2, 2)])
                    ea_pool.done(nc.gpsimd.tensor_copy(ecur[:, :, 1], dst_i[:, bass.ds(i * 2, 2)]), "idx")
                    ea_pool.wait(pool, i, "idx")
                    alone(pool)
                    for b in range(2):
                        for j in range(2):
                            nc.gpsimd.indirect_dma_start(
                                xe[:, b, j, :], None, a["x"], bass.IndirectOffsetOnAxis(ecur[:, b, j:j + 1], 0),
                                bounds_check=N - 1, oob_is_err=False).then_inc(s_gath, 16)

                pool.wait_ge(s_max, 4)
                nc.gpsimd.partition_all_reduce(emax[:, 1:2], emax[:, 0:1], P, RMAX).then_inc(s_max, 1)

                pool.wait_ge(s_table, 16 * table_dmas)
                with pool.Fori(0, ET // 2) as i:
                    for b in range(2):
                        eb_act.wait(pool, i, f"sum{b}")
                        eb_dve.wait(pool, i, "idx")
                        pool.wait_ge(s_scat[1 - b], (i + b) * 16)
                        alone(pool)
                        nc.gpsimd.indirect_dma_start(
                            agg, bass.IndirectOffsetOnAxis(eidx[:, b:b + 1], 0), esum[:, b, :], None,
                            bounds_check=NPAD - 1, oob_is_err=True, compute_op=ALU.add).then_inc(s_scat[b], 16)
                for b in range(2):
                    pool.wait_ge(s_scat[b], 16 * (ET // 2))

            @block.scalar
            def _(act):
                nc.scalar.preload_act_table_set("natural_log_exp_and_others")
                ea_act.start(act)
                eb_act.start(act)
                for tile, source in weight_loads:
                    act.dma_start(whole(tile), source).then_inc(s_weights, 16)
                act.dma_start(dt_w[2 * NS:2 * NS + RANK, :], a["dt_projT"]).then_inc(s_weights, 16)
                act.dma_start(ff1_b[:, :], a["ff1_b"].rearrange("(k p) -> p k", p=P)).then_inc(s_weights, 16)
                for i, name in col_loads:
                    act.dma_start(cols[:, i, :], a[name].rearrange("(k p) -> p k", p=P)).then_inc(s_weights, 16)
                for i, name in row_loads:
                    act.dma_start(rows[:, i, :], a[name].rearrange("(o n) -> o n", o=1)).then_inc(s_weights, 16)
                act.wait_ge(s_weights, 16 * N_LOADS)
                nc.scalar.activation(a_neg[:, :, :], a_neg[:, :, :], ACT.Exp).then_inc(s_prep_act, 1)
                act.wait_ge(s_prep_act, 1)
                nc.scalar.mul(a_neg[:, :, :], a_neg[:, :, :], -1.0).then_inc(s_prep_act, 1)
                act.wait_ge(s_prep_pe, 1)
                nc.scalar.copy(wa[:, :, :, :].rearrange("p k j h -> p (k j h)"),
                               ps_M[0][:, 0:HALVES * 2 * NH]).then_inc(s_prep_act, 1)
                act.wait_ge(s_prep_pe, 2)
                nc.scalar.copy(row_bc[:, 0:2, :].rearrange("p r n -> p (r n)"), ps_S[0][:, :])
                nc.scalar.copy(row_bc[:, 2, :], ps_S[1][:, 0:D]).then_inc(s_prep_act, 1)

                act.wait_ge(s_const, C_EPS)
                with act.Fori(0, ET // 2) as i:
                    ea_dve.wait(act, i, "aggr")
                    ea_act.done(nc.scalar.activation(ers[:, :], emv[:, :, 1], ACT.Ln, bias=eps_c[:, :]), "ln")
                    ea_act.wait(act, i, "ln")
                    ea_act.done(nc.scalar.activation(ers[:, :], ers[:, :], ACT.Exp, scale=-0.5), "rstd")
                    ea_dve.wait(act, i, "nmr")
                    for b in range(2):
                        ea_pe.wait(act, i - 1, f"T{b}")
                        for j in range(2):
                            last = nc.scalar.activation(he[:, b, j, :], xe[:, b, j, :], ACT.Relu,
                                                        bias=enm[:, 2 * b + j:2 * b + j + 1],
                                                        scale=ers[:, 2 * b + j:2 * b + j + 1])
                        ea_act.done(last, f"relu{b}")
                    for b in range(2):
                        ea_pe.wait(act, i, f"T{b}")
                        ea_act.done(nc.scalar.copy(heT[:, b, :, :, :].rearrange("p j k q -> p (j k q)"), ps_T[b][:, :]),
                                    f"hT{b}")
                    for b in range(2):
                        ea_pe.wait(act, i, f"mm{b}")
                        ea_act.done(nc.scalar.copy(proj[:, bass.ds(i * 2 + b, 1), :].rearrange("p o n -> p (o n)"),
                                                   ps_M[b][:, 0:AW]), f"proj{b}")

                act.wait_ge(s_max, 5)
                nc.scalar.mul(emax[:, 2:3], emax[:, 1:2], -1.0).then_inc(s_max, 1)
                act.wait_ge(s_max, 6)
                nc.scalar.activation(eexp[:, :, :], elog[:, :, :], ACT.Exp, bias=emax[:, 2:3]).then_inc(s_max, 1)

                with act.Fori(0, ET // 2) as i:
                    for b in range(2):
                        eb_pe.wait(act, i, f"sum{b}")
                        act.wait_ge(s_scat[b], i * 16)
                        eb_act.done(nc.scalar.copy(esum[:, b, :], ps_M[b][:, 0:AW]), f"sum{b}")

                turned = 0
                for s in plan:
                    old, new = KI[:, s["cur"], 1, :], KI[:, 1 - s["cur"], 1, :]
                    if s["kind"] == "stage":
                        act.wait_ge(s_sort, SORT0 + s["begin"])
                        act.wait_ge(s_turn_act, turned)
                        nc.scalar.copy(new, old).then_inc(s_icopy, 1)
                    if s["kind"] == "turn":
                        turned += 1
                        act.wait_ge(s_turn_pe, turned)
                        nc.scalar.copy(new, ps_S[1][:, :]).then_inc(s_turn_act, 1)

            @block.tensor
            def _(pe):
                ea_pe.start(pe)
                eb_pe.start(pe)
                pe.wait_ge(s_weights, 16 * N_LOADS)
                pe.wait_ge(s_const, C_SEL)
                for k in range(HALVES):
                    for r in range(HALVES):
                        last = nc.tensor.matmul(ps_M[0][:, k * 2 * NH:(k + 1) * 2 * NH],
                                                gat_wr[:, r, k * P:(k + 1) * P],
                                                a_blk[:, r, :, :].rearrange("p j h -> p (j h)"),
                                                start=(r == 0), stop=(r == HALVES - 1))
                last.then_inc(s_prep_pe, 1)
                nc.tensor.matmul(ps_S[0][:, :], ones_row[:, :], rows[:, 0:2, :].rearrange("p r n -> p (r n)"),
                                 start=True, stop=True)
                nc.tensor.matmul(ps_S[1][:, 0:D], ones_row[:, :], rows[:, 2, :], start=True, stop=True)\
                  .then_inc(s_prep_pe, 1)
                pe.wait_ge(s_prep_act, 4)
                nc.tensor.matmul(ps_deg[:, :], zeros_b[:, 0:P], zeros_b[:, :], start=True, stop=False)\
                  .then_inc(s_hist, 1)

                with pe.Fori(0, ET // 2) as i:
                    for b in range(2):
                        ea_act.wait(pe, i, f"relu{b}")
                        ea_act.wait(pe, i - 1, f"hT{b}")
                        for j in range(2):
                            for k in range(HALVES):
                                o = (j * HALVES + k) * P
                                last = nc.tensor.transpose(ps_T[b][:, o:o + P], he[:, b, j, k * P:(k + 1) * P],
                                                           ident[:, :])
                        ea_pe.done(last, f"T{b}")
                    for b in range(2):
                        ea_act.wait(pe, i, f"hT{b}")
                        ea_act.wait(pe, i - 1, f"proj{b}")
                        for k in range(HALVES):
                            nc.tensor.matmul(ps_M[b][:, 0:D], heT[:, b, 0, k, :], gat_wT[:, k, :],
                                             start=(k == 0), stop=(k == HALVES - 1))
                        for j in range(2):
                            for k in range(HALVES):
                                last = nc.tensor.matmul(ps_M[b][:, D:AW], heT[:, b, j, k, :], wa[:, k, j, :],
                                                        start=(j == 0 and k == 0), stop=(j == 1 and k == HALVES - 1))
                        ea_pe.done(last, f"mm{b}")
                    for b in range(2):
                        ea_dve.wait(pe, i, f"onehot{b}")
                        ea_pe.done(nc.tensor.matmul(ps_deg[:, :], oh_hi[:, b, :], oh_lo[:, b, :], start=False,
                                                    stop=False), f"hist{b}")
                nc.tensor.matmul(ps_deg[:, :], zeros_b[:, 0:P], zeros_b[:, :], start=False, stop=True)\
                  .then_inc(s_hist, 1)

                ea_act.wait(pe, ET // 2 - 1, "proj1")
                with pe.Fori(0, ET // 2) as i:
                    for b in range(2):
                        eb_dve.wait(pe, i, "dcb")
                        eb_dve.wait(pe, i - 1, f"same{b}")
                        eb_pe.done(nc.tensor.transpose(ps_T[b][:, 0:P], dcb[:, b, :], ident[:, :]), f"dT{b}")
                    for b in range(2):
                        eb_dve.wait(pe, i, "v")
                        eb_act.wait(pe, i - 1, f"sum{b}")
                        eb_pe.done(nc.tensor.matmul(ps_M[b][:, 0:AW], same[:, b, :], ev[:, b, :], start=True,
                                                    stop=True), f"sum{b}")

                turned = 0
                for s in [*plan, last_turn]:
                    if s["kind"] == "turn":
                        pe.wait_ge(s_sort, SORT0 + s["begin"])
                        pe.wait_ge(s_turn_act, turned)
                        for x in range(2):
                            for g in range(SUB):
                                last = nc.tensor.transpose(ps_S[x][:, g * P:(g + 1) * P],
                                                           KI[:, s["cur"], x, g * P:(g + 1) * P], ident[:, :])
                        last.then_inc(s_turn_pe, 1)
                        turned += 1

            @block.vector
            def _(dve):
                ea_dve.start(dve)
                eb_dve.start(dve)
                dve.wait_ge(s_edges, 16 * edge_dmas)
                dve.wait_ge(s_const, C_SEL)
                nc.vector.tensor_single_scalar(eidx_hi[:, :], src_i[:, :], 9, ALU.logical_shift_right)
                nc.vector.tensor_single_scalar(eidx_lo[:, :], src_i[:, :], CH - 1, ALU.bitwise_and)
                nc.vector.tensor_copy(dst_f[:, :], dst_i[:, :])
                nc.vector.tensor_scalar(pad_m[:, :], part_i[:, :], float(E), FAR, ALU.is_ge, ALU.mult)\
                  .then_inc(s_prep, 1)
                dve.wait_ge(s_prep, 1)
                nc.vector.tensor_copy(src_hi[:, :], eidx_hi[:, :])
                nc.vector.tensor_copy(src_lo[:, :], eidx_lo[:, :]).then_inc(s_prep, 1)
                dve.wait_ge(s_prep, 2)

                with dve.Fori(0, ET // 2) as i:
                    dve.wait_ge(s_gath, (i + 1) * 64)
                    ea_act.wait(dve, i - 1, "ln")
                    for q in range(4):
                        last = nc.vector.bn_stats(est[:, q, :], xe[:, q // 2, q % 2, :])
                    ea_dve.done(last, "stats")
                    ea_dve.wait(dve, i, "stats")
                    alone(dve)
                    for q in range(4):
                        last = nc.vector.bn_aggr(emv[:, q, :], est[:, q, :])
                    ea_dve.done(last, "aggr")
                    ea_act.wait(dve, i, "rstd")
                    ea_act.wait(dve, i - 1, "relu1")
                    ea_dve.done(nc.vector.scalar_tensor_tensor(enm[:, :], emv[:, :, 0], -1.0, ers[:, :], ALU.mult,
                                                               ALU.mult), "nmr")
                    for b in range(2):
                        ea_pe.wait(dve, i - 1, f"hist{b}")
                        t = i * 2 + b
                        nc.vector.tensor_scalar(oh_hi[:, b, :], iota_row[:, 0:P], src_hi[:, bass.ds(t, 1)], None,
                                                ALU.is_equal)
                        ea_dve.done(nc.vector.tensor_scalar(oh_lo[:, b, :], iota_row[:, :], src_lo[:, bass.ds(t, 1)],
                                                            None, ALU.is_equal), f"onehot{b}")

                ea_act.wait(dve, ET // 2 - 1, "proj1")
                logits = proj[:, :, D:AW]
                nc.vector.scalar_tensor_tensor(elog[:, :, :], logits, 0.2, logits, ALU.mult, ALU.max)\
                  .then_inc(s_max, 1)
                dve.wait_ge(s_max, 1)
                nc.vector.tensor_tensor(elog[:, :, :], elog[:, :, :],
                                        pad_m[:, :].unsqueeze(2).broadcast_to([P, ET, NH]), ALU.add).then_inc(s_max, 1)
                dve.wait_ge(s_max, 2)
                nc.vector.reduce_max(emax[:, 0:1], elog[:, :, :].rearrange("p t h -> p (t h)"), AX_X)\
                  .then_inc(s_max, 2)

                dve.wait_ge(s_max, 7)
                with dve.Fori(0, ET // 2) as i:
                    eb_pe.wait(dve, i - 1, "dT1")
                    for b in range(2):
                        last = nc.vector.tensor_scalar(dcb[:, b, :], zeros[:, 0:P], dst_f[:, bass.ds(i * 2 + b, 1)],
                                                       None, ALU.add)
                    eb_dve.done(last, "dcb")
                    for b in range(2):
                        eb_pe.wait(dve, i, f"dT{b}")
                        eb_pe.wait(dve, i - 1, f"sum{b}")
                        eb_dve.done(nc.vector.tensor_scalar(same[:, b, :], ps_T[b][:, 0:P],
                                                            dst_f[:, bass.ds(i * 2 + b, 1)], None, ALU.is_equal),
                                    f"same{b}")
                    eb_dve.wait(dve, i, "same1")
                    for b in range(2):
                        last = nc.vector.tensor_tensor_reduce(junk[:, b, :], same[:, b, :], low_tri[:, :], 1.0, 0.0,
                                                              ALU.mult, ALU.add, cnt[:, b:b + 1])
                    eb_dve.done(last, "cnt")
                    pair = dst_f[:, bass.ds(i * 2, 2)]
                    eb_dve.done(nc.vector.tensor_scalar(gap[:, :], pair, -1.0, dump_f[:, :], ALU.mult, ALU.add), "gap")
                    eb_dve.wait(dve, i, "gap")
                    eb_dve.done(nc.vector.scalar_tensor_tensor(pick[:, :], cnt[:, :], 1.0, gap[:, :], ALU.min,
                                                               ALU.mult), "pick")
                    eb_dve.wait(dve, i, "pick")
                    for b in range(2):
                        dve.wait_ge(s_scat[b], i * 16)
                    eb_dve.done(nc.vector.tensor_tensor(eidx[:, :], pick[:, :], pair, ALU.add), "idx")
                    nc.vector.tensor_tensor(ev[:, :, 0:D].rearrange("p t (h f) -> p t h f", h=NH),
                                            proj[:, bass.ds(i * 2, 2), 0:D].rearrange("p t (h f) -> p t h f", h=NH),
                                            eexp[:, bass.ds(i * 2, 2), :].unsqueeze(3).broadcast_to([P, 2, NH, FOUT]),
                                            ALU.mult)
                    eb_dve.done(nc.vector.tensor_copy(ev[:, :, D:AW], eexp[:, bass.ds(i * 2, 2), :]), "v")

                ops = 0

                def step(ins):
                    nonlocal ops
                    ops += 1
                    ins.then_inc(s_sort, 1)

                nc.vector.tensor_single_scalar(sgn_i[:, :], pl_i[:, :], 1, ALU.logical_shift_right)\
                  .then_inc(s_sort, 1)
                ops += 1
                dve.wait_ge(s_sort, ops)
                step(nc.vector.tensor_tensor(gray[:, :], pl_i[:, :], sgn_i[:, :], ALU.bitwise_xor))
                dve.wait_ge(s_hist, 2)
                dve.wait_ge(s_noise, 16 * noise_dmas)
                step(nc.vector.tensor_tensor(KI[:, 0, 0, :], KI[:, 0, 0, :], ps_deg[:, :], ALU.add))
                assert ops == SORT0
                staged = turned = 0
                for s in plan:
                    old, new = KI[:, s["cur"], :, :], KI[:, 1 - s["cur"], :, :]
                    assert ops == SORT0 + s["begin"]
                    dve.wait_ge(s_sort, ops)
                    if s["kind"] == "sign":
                        k = s["k"]
                        bits, shift = (pl_i, 1) if k == 1 else (gray, k - 1)
                        dve.wait_ge(s_icopy, staged)
                        step(nc.vector.tensor_scalar(sgn_i[:, :], bits[:, :], shift, 1, ALU.logical_shift_right,
                                                     ALU.bitwise_and))
                        dve.wait_ge(s_sort, ops)
                        step(nc.vector.tensor_scalar(sgn[:, :], sgn_i[:, :], -2.0, 1.0, ALU.mult, ALU.add))
                        dve.wait_ge(s_sort, ops)
                        step(nc.vector.tensor_tensor(old, old, sgn[:, :].unsqueeze(1).broadcast_to([P, 2, CH]),
                                                     ALU.mult))
                    if s["kind"] == "turn":
                        turned += 1
                        dve.wait_ge(s_turn_pe, turned)
                        step(nc.vector.tensor_copy(new[:, 0, :], ps_S[0][:, :]))
                        dve.wait_ge(s_turn_act, turned)
                    if s["kind"] == "stage":
                        d = s["dist"]

                        def sides(ap):
                            v = ap.rearrange("p x (g two d) -> p x g two d", two=2, d=d)
                            return v[:, :, :, 0, :], v[:, :, :, 1, :]

                        def half(ap):
                            return ap.rearrange("p (g d) -> p g d", d=d)

                        (oa, ob), (na, nb) = sides(old), sides(new)
                        ge = cmp_ge[:, :, :].rearrange("p x (g d) -> p x g d", d=d)
                        step(nc.vector.tensor_tensor(ge, oa, ob, ALU.is_ge))
                        step(nc.vector.tensor_tensor(half(cmp_le[:, :]), oa[:, 0], ob[:, 0], ALU.is_le))
                        step(nc.vector.tensor_tensor(na[:, 0], oa[:, 0], ob[:, 0], ALU.min))
                        dve.wait_ge(s_sort, ops - 2)
                        step(nc.vector.tensor_tensor(cmp_w[:, :], cmp_ge[:, 0, :], cmp_ge[:, 1, :], ALU.add))
                        step(nc.vector.tensor_tensor(nb[:, 0], oa[:, 0], ob[:, 0], ALU.max))
                        dve.wait_ge(s_sort, ops - 1)
                        step(nc.vector.tensor_tensor(swap[:, :], cmp_w[:, :], cmp_le[:, :], ALU.is_gt))
                        staged += 1
                        dve.wait_ge(s_sort, ops)
                        dve.wait_ge(s_icopy, staged)
                        step(nc.vector.copy_predicated(na[:, 1], half(swap[:, :]), ob[:, 1]))
                        step(nc.vector.copy_predicated(nb[:, 1], half(swap[:, :]), oa[:, 1]))
                dve.wait_ge(s_turn_pe, turned + 1)
                nc.vector.tensor_copy(perm[:, :, :].rearrange("p s c -> p (s c)"), ps_S[1][:, :]).then_inc(s_prep, 1)
                dve.wait_ge(s_prep, 3)

        NRING = 3
        X = sb("X", [P, NRING, SUB, D])
        H0 = sb("H0", [P, NRING, SUB, D])
        idx = sb("idx", [P, NRING, SUB], I32)
        XS = sb("XS", [P, NRING, 2 * HALVES, CH])
        DT = sb("DT", [P, NRING, HALVES, CH])
        DTX = sb("DTX", [P, NRING, HALVES, CH])
        BC3 = sb("BC3", [3 * 2 * NS, NRING, CH], BF16)
        H0T = sb("H0T", [P, HALVES, CH])
        XCP = sb("XCP", [P, HALVES, TAPS - 1 + CH])
        AZ = sb("AZ", [P, 2 * HALVES, CH])
        EX = sb("EX", [P, 2 * HALVES, CH])
        R1 = sb("R1", [2 * NS, CH])
        MID = sb("MID", [2 * NS, CH], BF16)
        DTR = sb("DTR", [2 * NS + RANK, CH])
        st_p = sb("st_p", [P, SUB, 6])
        mv_p = sb("mv_p", [P, SUB, 2])
        rs_p = sb("rs_p", [P, SUB])
        nm_p = sb("nm_p", [P, SUB])
        BS = sb("BS", [P, 2, CH])
        DB = sb("DB", [P, 2, HALVES, CH])
        HS = sb("HS", [P, 2, HALVES, CH])
        GS = sb("GS", [P, 2, HALVES, CH])
        last_h = sb("last_h", [P, NS, HALVES])
        AG = sb("AG", [P, SUB, AW])
        XB = sb("XB", [P, SUB, D])
        F1 = sb("F1", [P, FF // P, CH])
        YV = F1[:, 0:HALVES, :]
        HG = F1[:, HALVES:, :].rearrange("p h (u n) -> p (h u) n", n=D)
        RS = sb("RS", [P, SUB, D])
        DIFF = RS[:, :, :].rearrange("p (h u) n -> p h (u n)", h=HALVES)
        LV = sb("LV", [P, SUB, D])
        OUT = LV
        LM = sb("LM", [P, SUB, D])
        GT = LM[:, :, :].rearrange("p (h u) n -> p h (u n)", h=HALVES)
        HAT = sb("HAT", [P, HALVES, CH])
        HLT = sb("HLT", [P, HALVES, CH])
        rden = sb("rden", [P, SUB, NH])
        st_o = sb("st_o", [P, SUB, 6])
        mv_o = sb("mv_o", [P, SUB, 2])
        rs_o = sb("rs_o", [P, SUB])
        nm_o = sb("nm_o", [P, SUB])

        PSY = ctx.enter_context(nc.psum_tensor("PSY", [P, HALVES, CH], F32))
        PSA = ctx.enter_context(nc.psum_tensor("PSA", [P, HALVES, CH], F32))
        PSB = ctx.enter_context(nc.psum_tensor("PSB", [P, CH], F32))
        PSC = ctx.enter_context(nc.psum_tensor("PSC", [P, CH], F32))
        PSW = [ctx.enter_context(nc.psum_tensor(f"PSW{i}", [P, CH], F32)) for i in range(2)]

        s_x = sem("s_x")
        s_ag = sem("s_ag")
        s_out = sem("s_out")
        s_main = sem("s_main")
        r_pool = Steps(sem("r_pool"), "idx tu series")
        r_act = Steps(sem("r_act"), "ln rstd relu h0T0 h0T1 in0 in1 in2 in3 silu dtr abs0 rel0 abs1 rel1 u w sq t L")
        r_dve = Steps(sem("r_dve"), "stats aggr nmr carry c0 c1 c2 c3 hi r1 mid mids lo corr lsum small pick dt dtx")
        r_pe = Steps(sem("r_pe"), "h0T0 h0T1 in0 in1 in2 in3 dbc dt0 dt1")
        DVE_B = [n for n in range(NS) if n % 4 == 2]
        POOL_B = [n for n in range(NS) if n not in DVE_B]

        def states(*names, of=range(NS)):
            return " ".join(f"{x}{n}" for n in of for x in names)


        c_pe_b = Steps(sem("c_pe_b"), states("B"))
        c_pe_c = Steps(sem("c_pe_c"), states("C"))
        c_pe_y = Steps(sem("c_pe_y"), states("y"))
        c_act_b = Steps(sem("c_act_b"), states("B", of=POOL_B))
        c_act_a = Steps(sem("c_act_a"), states("a0_", "a1_"))
        c_db_pool = Steps(sem("c_db_pool"), states("db", of=POOL_B))
        c_db_dve = Steps(sem("c_db_dve"), states("db", of=DVE_B))
        c_dve = Steps(sem("c_dve"), states("s0_", "s1_", "last", "g"))
        o_pool = Steps(sem("o_pool"), "hg xb diff")
        o_act = Steps(sem("o_act"), "lnA rsA nrA elu hAT0 hAT1 lnL rsL nrL hLT0 hLT1 g0 g1 f0 f1 f2 f3 ln2 rs2 nr2")
        o_dve = Steps(sem("o_dve"), "y2 y3 res0 res1 stA agA nmA den rden loc locs mn elu stL agL nmL"
                                    " gm h st2a st2b ag2 nm2 fg fo")
        o_pe = Steps(sem("o_pe"), "out0 out1 hAT0 hAT1 hLT0 hLT1 gate0 gate1 ff1_0 ff1_1 ff1_2 ff1_3 ff2_0 ff2_1")

        PRE, POST = "pre", "post"
        uses = [
            (1, POST, "out0", o_dve, "res0"), (1, POST, "out1", o_dve, "res1"),
            (4, POST, "hAT0", o_act, "hAT0"), (4, POST, "hAT1", o_act, "hAT1"),
            (4, PRE, "h0T0", r_act, "h0T0"), (4, PRE, "h0T1", r_act, "h0T1"),
            (5, PRE, "in0", r_act, "in0"), (5, PRE, "in1", r_act, "in1"),
            (6, POST, "hLT0", o_act, "hLT0"), (6, POST, "hLT1", o_act, "hLT1"),
            (6, PRE, "in2", r_act, "in2"), (6, PRE, "in3", r_act, "in3"),
            (7, POST, "gate0", o_act, "g0"), (8, POST, "gate1", o_act, "g1"),
            (9, PRE, "dbc", r_dve, "r1"),
            (10, PRE, "dt0", r_act, "rel0"), (10, PRE, "dt1", r_act, "rel1"),
            (11, POST, "ff1_0", o_act, "f0"), (11, POST, "ff1_1", o_act, "f1"),
            (12, POST, "ff1_2", o_act, "f2"), (12, POST, "ff1_3", o_act, "f3"),
            (13, POST, "ff2_0", o_act, "nr2"), (14, POST, "ff2_1", o_act, "nr2"),
        ]

        def bank(section, what):
            return [u[1:3] for u in uses].index((section, what)) % 2

        block = ctx.enter_context(nc.Block())

        def periods(eng, slot):
            def period(c, r, pre, scan, post):
                for n in range(NS):
                    slot(c, r, n, pre, scan, post)
            period(-1, NRING - 1, True, False, False)
            period(0, 0, True, True, False)
            with eng.Fori(0, (NC - 2) // 3) as i:
                for j in range(3):
                    period(i * 3 + (1 + j), (1 + j) % NRING, True, True, True)
            period(NC - 1, (NC - 1) % NRING, False, True, True)
            period(NC, NC % NRING, False, False, True)

        def rings(r):
            return (r + 1) % NRING, r, (r - 1) % NRING

        def back(c, n, k):
            return (c, n - k) if n >= k else (c - 1, n - k + NS)

        def wait_db(eng, c, n):
            (c_db_dve if n in DVE_B else c_db_pool).wait(eng, c, f"db{n}")

        def leads(n, pre, scan):
            return (scan and n < NS - 1) or (pre and n == NS - 1)

        def after(c, n, rp, rs):
            return (c, n + 1, rs) if n < NS - 1 else (c + 1, 0, rp)

        @block.gpsimd
        def _(pool):
            for st in (r_pool, o_pool):
                st.start(pool)
            c_db_pool.start(pool)
            nc.gpsimd.memset(one_c[:, :], 1.0)
            nc.gpsimd.memset(mhalf_c[:, :], -0.5)
            nc.gpsimd.memset(last_h[:, :, :], 0.0)
            nc.gpsimd.memset(XCP[:, :, :], 0.0)
            nc.gpsimd.memset(X[:, :, :, :], 0.0)
            nc.gpsimd.memset(AG[:, :, :], 0.0).then_inc(s_main, 1)
            pool.wait_ge(s_main, 1)

            def gather(dst, table, r, s, bound):
                return nc.gpsimd.indirect_dma_start(dst, None, table, bass.IndirectOffsetOnAxis(idx[:, r, s:s + 1], 0),
                                                    bounds_check=bound, oob_is_err=False)

            def slot(c, r, n, pre, scan, post):
                rp, rs, ro = rings(r)
                if leads(n, pre, scan):
                    c1, n1, r1 = after(c, n, rp, rs)
                    if n1 in POOL_B:
                        if n1 == 0:
                            r_dve.wait(pool, c1, "dtx")
                        c_act_b.wait(pool, c1, f"B{n1}")
                        cb, nb = back(c1, n1, 2)
                        c_dve.wait(pool, cb, f"s1_{nb}")
                        alone(pool)
                        c_db_pool.done(nc.gpsimd.tensor_tensor(
                            DB[:, n1 % 2, :, :], DTX[:, r1, :, :],
                            BS[:, n1 % 2, :].unsqueeze(1).broadcast_to([P, HALVES, CH]), ALU.mult), f"db{n1}")
                if n == 0 and pre:
                    o_dve.wait(pool, c - 2, "fo")
                    o_pool.wait(pool, c - 2, "xb")
                    if post:
                        pool.wait_ge(s_out, (c - 1) * (16 * SUB))
                    r_pool.done(nc.gpsimd.tensor_copy(idx[:, rp, :].rearrange("p (s o) -> p s o", o=1),
                                                      perm[:, :, bass.ds(c + 1, 1)]), "idx")
                    r_pool.wait(pool, c + 1, "idx")
                    alone(pool)
                    for s in range(SUB):
                        gather(X[:, rp, s, :], a["x"], rp, s, N - 1).then_inc(s_x, 16)
                if n == 1 and post:
                    o_dve.wait(pool, c - 2, "loc")
                    alone(pool)
                    for s in range(SUB):
                        gather(AG[:, s, :], agg, ro, s, N - 1).then_inc(s_ag, 16)
                if n == 2 and post:
                    o_dve.wait(pool, c - 2, "locs")
                    alone(pool)
                    o_pool.done(nc.gpsimd.tensor_tensor(HG[:, :, :], H0[:, ro, :, :],
                                                        row_bc[:, GATB, :].unsqueeze(1).broadcast_to([P, SUB, D]),
                                                        ALU.add), "hg")
                if n == 4 and post:
                    o_dve.wait(pool, c - 2, "fo")
                    alone(pool)
                    o_pool.done(nc.gpsimd.tensor_tensor(XB[:, :, :], X[:, ro, :, :],
                                                        row_bc[:, LN2B, :].unsqueeze(1).broadcast_to([P, SUB, D]),
                                                        ALU.add), "xb")
                if n == 7 and post:
                    o_act.wait(pool, c - 1, "hLT1")
                    o_dve.wait(pool, c - 2, "gm")
                    alone(pool)
                    o_pool.done(nc.gpsimd.tensor_tensor(DIFF[:, :, :], HLT[:, :, :], HAT[:, :, :], ALU.subtract), "diff")
                if n == 11 and pre:
                    r_act.wait(pool, c + 1, "t")
                    alone(pool)
                    r_pool.done(nc.gpsimd.tensor_tensor(DT[:, rp, :, :], DT[:, rp, :, :], DTX[:, rp, :, :], ALU.mult), "tu")
                    r_pool.wait(pool, c + 1, "tu")
                    alone(pool)
                    r_pool.done(nc.gpsimd.tensor_tensor(DT[:, rp, :, :], DT[:, rp, :, :], EX[:, 0:2, :], ALU.add), "series")
                if n == NS - 1 and post:
                    o_dve.wait(pool, c - 1, "fo")
                    alone(pool)
                    for s in range(SUB):
                        nc.gpsimd.indirect_dma_start(
                            out, bass.IndirectOffsetOnAxis(idx[:, ro, s:s + 1], 0), OUT[:, s, :], None,
                            bounds_check=N - 1, oob_is_err=False).then_inc(s_out, 16)

            periods(pool, slot)
            pool.wait_ge(s_out, NC * SUB * 16)

        @block.scalar
        def _(act):
            nc.scalar.preload_act_table_set("natural_log_exp_and_others")
            for st in (r_act, c_act_b, c_act_a, o_act):
                st.start(act)

            def slot(c, r, n, pre, scan, post):
                rp, rs, ro = rings(r)
                cp, co = c + 1, c - 1
                if scan:
                    for h in range(HALVES):
                        cb, nb = back(c, n, 1)
                        c_dve.wait(act, cb, f"s{h}_{nb}")
                        if n == 0 and h == 0:
                            r_dve.wait(act, c, "dt")
                        c_act_a.done(nc.scalar.activation(PSA[:, h, :], DT[:, rs, h, :], ACT.Exp,
                                                          scale=a_neg[:, h, n:n + 1]), f"a{h}_{n}")
                if leads(n, pre, scan):
                    c1, n1, _ = after(c, n, rp, rs)
                    if n1 in POOL_B:
                        c_pe_b.wait(act, c1, f"B{n1}")
                        wait_db(act, *back(c1, n1, 2))
                        if n1 - 2 in DVE_B:
                            wait_db(act, *back(c1, n1, 4))
                        c_act_b.done(nc.scalar.copy(BS[:, n1 % 2, :], PSB[:, :]), f"B{n1}")
                if n == 8 and (pre or post):
                    nc.scalar.preload_act_table_set("silu_and_others")
                    if pre:
                        r_dve.wait(act, cp, "c3")
                        r_act.wait(act, cp, "in3")
                        r_act.done(nc.scalar.activation(XS[:, rp, :, :], AZ[:, :, :], ACT.Silu), "silu")
                    if post:
                        for h in range(HALVES):
                            o_pe.wait(act, co, f"gate{h}")
                            if h == 0:
                                o_dve.wait(act, c - 2, "h")
                            o_act.done(nc.scalar.activation(GT[:, h, :], PSW[bank(POST, f"gate{h}")][:, :], ACT.Tanh,
                                                            scale=0.5), f"g{h}")
                    nc.scalar.preload_act_table_set("natural_log_exp_and_others")
                if post:
                    if n == 2:
                        o_dve.wait(act, co, "agA")
                        o_act.done(nc.scalar.activation(rs_o[:, :], mv_o[:, :, 1], ACT.Ln, bias=eps_c[:, :]), "lnA")
                        o_act.wait(act, co, "lnA")
                        o_act.done(nc.scalar.activation(rs_o[:, :], rs_o[:, :], ACT.Exp, scale=-0.5), "rsA")
                    if n == 3:
                        o_dve.wait(act, co, "nmA")
                        for s in range(SUB):
                            last = nc.scalar.activation(RS[:, s, :], RS[:, s, :], ACT.Identity,
                                                        bias=nm_o[:, s:s + 1], scale=rs_o[:, s:s + 1])
                        o_act.done(last, "nrA")
                        o_dve.wait(act, co, "mn")
                        o_act.done(nc.scalar.activation(LM[:, :, :], LM[:, :, :], ACT.Exp), "elu")
                    if n == 4:
                        for h in range(HALVES):
                            o_pe.wait(act, co, f"hAT{h}")
                            if h == 0:
                                o_pe.wait(act, c - 2, "ff2_1")
                            o_act.done(nc.scalar.activation(HAT[:, h, :], PSW[bank(POST, f"hAT{h}")][:, :], ACT.Identity,
                                                            bias=cols[:, LGB, h:h + 1], scale=cols[:, LGG, h:h + 1]),
                                       f"hAT{h}")
                    if n == 4:
                        o_dve.wait(act, co, "agL")
                        o_act.done(nc.scalar.activation(rs_o[:, :], mv_o[:, :, 1], ACT.Ln, bias=eps_c[:, :]), "lnL")
                        o_act.wait(act, co, "lnL")
                        o_act.done(nc.scalar.activation(rs_o[:, :], rs_o[:, :], ACT.Exp, scale=-0.5), "rsL")
                    if n == 5:
                        o_dve.wait(act, co, "nmL")
                        for s in range(SUB):
                            last = nc.scalar.activation(LV[:, s, :], LV[:, s, :], ACT.Identity,
                                                        bias=nm_o[:, s:s + 1], scale=rs_o[:, s:s + 1])
                        o_act.done(last, "nrL")
                    if n == 6:
                        for h in range(HALVES):
                            o_pe.wait(act, co, f"hLT{h}")
                            if h == 0:
                                o_pe.wait(act, c - 2, "gate1")
                                o_pool.wait(act, c - 2, "diff")
                            o_act.done(nc.scalar.activation(HLT[:, h, :], PSW[bank(POST, f"hLT{h}")][:, :], ACT.Identity,
                                                            bias=cols[:, LLB, h:h + 1], scale=cols[:, LLG, h:h + 1]),
                                       f"hLT{h}")
                    if n in (11, 12):
                        for m in (2 * (n - 11), 2 * (n - 11) + 1):
                            o_pe.wait(act, co, f"ff1_{m}")
                            if m == 0:
                                o_pe.wait(act, c - 2, "ff2_1")
                            o_act.done(nc.scalar.activation(F1[:, m, :], PSW[bank(POST, f"ff1_{m}")][:, :], ACT.Relu,
                                                            bias=ff1_b[:, m:m + 1]), f"f{m}")
                    if n == 14:
                        o_dve.wait(act, co, "ag2")
                        o_act.done(nc.scalar.activation(rs_o[:, :], mv_o[:, :, 1], ACT.Ln, bias=eps_c[:, :]), "ln2")
                        o_act.wait(act, co, "ln2")
                        o_act.done(nc.scalar.activation(rs_o[:, :], rs_o[:, :], ACT.Exp, scale=-0.5), "rs2")
                        o_dve.wait(act, co, "nm2")
                        for s in range(SUB):
                            w = PSW[bank(POST, f"ff2_{s // 2}")]
                            last = nc.scalar.activation(OUT[:, s, :], w[:, s % 2 * D:s % 2 * D + D], ACT.Identity,
                                                        bias=nm_o[:, s:s + 1], scale=rs_o[:, s:s + 1])
                        o_act.done(last, "nr2")
                if pre:
                    if n == 2:
                        r_dve.wait(act, cp, "aggr")
                        r_act.done(nc.scalar.activation(rs_p[:, :], mv_p[:, :, 1], ACT.Ln, bias=eps_c[:, :]), "ln")
                        r_act.wait(act, cp, "ln")
                        r_act.done(nc.scalar.activation(rs_p[:, :], rs_p[:, :], ACT.Exp, scale=-0.5), "rstd")
                    if n == 3:
                        r_dve.wait(act, cp, "nmr")
                        o_dve.wait(act, c - 2, "res1")
                        o_pool.wait(act, c - 2, "hg")
                        for s in range(SUB):
                            last = nc.scalar.activation(H0[:, rp, s, :], X[:, rp, s, :], ACT.Relu,
                                                        bias=nm_p[:, s:s + 1], scale=rs_p[:, s:s + 1])
                        r_act.done(last, "relu")
                    if n == 4:
                        for h in range(HALVES):
                            r_pe.wait(act, cp, f"h0T{h}")
                            if h == 0:
                                r_pe.wait(act, c, "in3")
                            r_act.done(nc.scalar.copy(H0T[:, h, :], PSW[bank(PRE, f"h0T{h}")][:, :]), f"h0T{h}")
                    if n == 5:
                        for h in range(HALVES):
                            r_pe.wait(act, cp, f"in{h}")
                            r_dve.wait(act, cp, "carry")
                            r_act.done(nc.scalar.copy(XCP[:, h, TAPS - 1:], PSW[bank(PRE, f"in{h}")][:, :]), f"in{h}")
                    if n == 6:
                        for h in range(2, 2 + HALVES):
                            r_pe.wait(act, cp, f"in{h}")
                            r_dve.wait(act, c, "dt")
                            r_act.done(nc.scalar.copy(AZ[:, h, :], PSW[bank(PRE, f"in{h}")][:, :]), f"in{h}")
                    if n == 9:
                        r_pe.wait(act, cp, "dbc")
                        r_pe.wait(act, c, "dt1")
                        r_act.done(nc.scalar.copy(DTR[2 * NS:, :], PSW[bank(PRE, "dbc")][2 * NS:2 * NS + RANK, :]), "dtr")
                    if n == 10:
                        for h in range(HALVES):
                            r_pe.wait(act, cp, f"dt{h}")
                            if h == 0:
                                r_dve.wait(act, c, "dt")
                            w = PSW[bank(PRE, f"dt{h}")][:, :]
                            r_act.done(nc.scalar.activation(EX[:, h, :], w, ACT.Abs, bias=cols[:, DTB, h:h + 1]),
                                       f"abs{h}")
                            r_act.done(nc.scalar.activation(EX[:, 2 + h, :], w, ACT.Relu, bias=cols[:, DTB, h:h + 1]),
                                       f"rel{h}")
                        r_act.wait(act, cp, "abs1")
                        r_act.done(nc.scalar.activation(EX[:, 0:2, :], EX[:, 0:2, :], ACT.Exp, scale=-1.0), "u")
                        r_act.wait(act, cp, "u")
                        r_act.done(nc.scalar.activation(AZ[:, 2:4, :], EX[:, 0:2, :], ACT.Identity, bias=one_c[:, :]), "w")
                        r_act.done(nc.scalar.activation(DTX[:, rp, :, :], EX[:, 0:2, :], ACT.Square), "sq")
                        r_act.done(nc.scalar.activation(DT[:, rp, :, :], EX[:, 0:2, :], ACT.Identity, scale=1.0 / 3,
                                                        bias=mhalf_c[:, :]), "t")
                        r_act.done(nc.scalar.activation(AZ[:, 0:2, :], EX[:, 0:2, :], ACT.Ln, bias=1.0), "L")

            periods(act, slot)

        @block.tensor
        def _(pe):
            for st in (r_pe, c_pe_b, c_pe_c, c_pe_y, o_pe):
                st.start(pe)

            def broadcast(ps, r, row):
                return nc.tensor.matmul(ps[:, :], sel[:, row, :], BC3[:, r, :], start=True, stop=True)

            def sum_y(c, n):
                c_dve.wait(pe, c, f"g{n}")
                if n == 0:
                    o_dve.wait(pe, c - 1, "y2")
                for h in range(HALVES):
                    last = nc.tensor.matmul(PSY[:, h, :], ident[:, :], GS[:, n % 2, h, :], start=(n == 0),
                                            stop=(n == NS - 1))
                c_pe_y.done(last, f"y{n}")

            def free_bank(u, c, pre, scan, post):
                kinds = {PRE: 1, POST: -1}
                for v in range(u - 2, -1, -2):
                    if (pre if uses[v][1] == PRE else post):
                        uses[v][3].wait(pe, c + kinds[uses[v][1]], uses[v][4])
                        return
                same_bank = [v for v in range(len(uses)) if v % 2 == u % 2]
                for v in reversed(same_bank):
                    if uses[v][1] == POST or scan or pre:
                        uses[v][3].wait(pe, c - 1 + kinds[uses[v][1]], uses[v][4])
                        return

            def slot(c, r, n, pre, scan, post):
                rp, rs, ro = rings(r)
                cp, co = c + 1, c - 1
                if leads(n, pre, scan):
                    c1, n1, r1 = after(c, n, rp, rs)
                    cb, nb = back(c1, n1, 1)
                    if nb in DVE_B:
                        c_db_dve.wait(pe, cb, f"db{nb}")
                    else:
                        c_act_b.wait(pe, cb, f"B{nb}")
                    if n1 == 0:
                        r_dve.wait(pe, c1, "lo")
                    c_pe_b.done(broadcast(PSB, r1, n1), f"B{n1}")
                if scan:
                    cb, nb = back(c, n, 1)
                    c_dve.wait(pe, cb, f"g{nb}")
                    c_pe_c.done(broadcast(PSC, rs, NS + n), f"C{n}")
                    if n > 0:
                        sum_y(c, n - 1)
                if n == 0 and post:
                    sum_y(co, NS - 1)
                for u, (at, section, what, _, _) in enumerate(uses):
                    if at != n or not (pre if section == PRE else post):
                        continue
                    w = PSW[u % 2]
                    h = int(what[-1]) if what[-1].isdigit() else 0
                    free_bank(u, c, pre, scan, post)
                    if what.startswith("out"):
                        o_dve.wait(pe, co, "y3")
                        for s in (2 * h, 2 * h + 1):
                            for k in range(HALVES):
                                last = nc.tensor.matmul(w[:, s % 2 * D:s % 2 * D + D], YV[:, k, s * P:(s + 1) * P],
                                                        out_w[:, k, :], start=(k == 0), stop=(k == HALVES - 1))
                        o_pe.done(last, what)
                    if what.startswith("hAT") or what.startswith("hLT"):
                        src_t = RS if what.startswith("hAT") else LV
                        o_act.wait(pe, co, "nrA" if what.startswith("hAT") else "nrL")
                        for s in range(SUB):
                            last = nc.tensor.transpose(w[:, s * P:(s + 1) * P], src_t[:, s, h * P:(h + 1) * P],
                                                       ident[:, :])
                        o_pe.done(last, what)
                    if what.startswith("gate"):
                        o_act.wait(pe, co, "hLT1")
                        for j, (wt, act_t) in enumerate(((wl_w, HLT), (wg_w, HAT))):
                            for k in range(HALVES):
                                last = nc.tensor.matmul(w[:, :], wt[:, k, h * P:(h + 1) * P], act_t[:, k, :],
                                                        start=(j == 0 and k == 0), stop=(j == 1 and k == HALVES - 1))
                        o_pe.done(last, what)
                    if what.startswith("ff1"):
                        o_dve.wait(pe, co, "h")
                        for k in range(HALVES):
                            last = nc.tensor.matmul(w[:, :], ff1_w[:, k, h * P:(h + 1) * P], HAT[:, k, :],
                                                    start=(k == 0), stop=(k == HALVES - 1))
                        o_pe.done(last, what)
                    if what.startswith("ff2"):
                        o_act.wait(pe, co, "f3")
                        for s in (2 * h, 2 * h + 1):
                            cols_s = slice(s % 2 * D, s % 2 * D + D)
                            for k in range(FF // P):
                                nc.tensor.matmul(w[:, cols_s], F1[:, k, s * P:(s + 1) * P], ff2_w[:, k, :],
                                                 start=(k == 0), stop=False)
                            nc.tensor.matmul(w[:, cols_s], ones_row[:, :], rows[:, FF2B, :], start=False, stop=False)
                            for k in range(HALVES):
                                o = s % 2 * D + k * P
                                last = nc.tensor.matmul(w[:, o:o + P], HAT[:, k, s * P:(s + 1) * P], ident[:, :],
                                                        start=False, stop=(k == HALVES - 1))
                        o_pe.done(last, what)
                    if what.startswith("h0T"):
                        r_act.wait(pe, cp, "relu")
                        for s in range(SUB):
                            last = nc.tensor.transpose(w[:, s * P:(s + 1) * P], H0[:, rp, s, h * P:(h + 1) * P],
                                                       ident[:, :])
                        r_pe.done(last, what)
                    if what.startswith("in"):
                        r_act.wait(pe, cp, "h0T1")
                        for k in range(HALVES):
                            last = nc.tensor.matmul(w[:, :], in_w[:, k, h * P:(h + 1) * P], H0T[:, k, :],
                                                    start=(k == 0), stop=(k == HALVES - 1))
                        r_pe.done(last, what)
                    if what == "dbc":
                        r_act.wait(pe, cp, "silu")
                        for k in range(HALVES):
                            last = nc.tensor.matmul(w[0:2 * NS + RANK, :], xp_w[:, k, :], XS[:, rp, k, :],
                                                    start=(k == 0), stop=(k == HALVES - 1))
                        r_pe.done(last, what)
                    if what in ("dt0", "dt1"):
                        r_act.wait(pe, cp, "dtr")
                        r_pe.done(nc.tensor.matmul(w[:, :], dt_w[2 * NS:, h * P:(h + 1) * P], DTR[2 * NS:, :],
                                                   start=True, stop=True), what)

            periods(pe, slot)

        @block.vector
        def _(dve):
            for st in (r_dve, c_dve, c_db_dve, o_dve):
                st.start(dve)
            dve.wait_ge(s_main, 1)

            def stats(st, rows_of, tile_s, tile_m, c, names):
                for s in range(SUB):
                    last = nc.vector.bn_stats(tile_s[:, s, :], rows_of(s))
                st.done(last, names[0])
                st.wait(dve, c, names[0])
                alone(dve)
                for s in range(SUB):
                    last = nc.vector.bn_aggr(tile_m[:, s, :], tile_s[:, s, :])
                st.done(last, names[1])

            def slot(c, r, n, pre, scan, post):
                rp, rs, ro = rings(r)
                cp, co = c + 1, c - 1
                if scan:
                    wait_db(dve, c, n)
                    for h in range(HALVES):
                        c_act_a.wait(dve, c, f"a{h}_{n}")
                        c_dve.wait(dve, c - 1, f"last{n}")
                        c_dve.done(nc.vector.tensor_tensor_scan(HS[:, n % 2, h, :], PSA[:, h, :], DB[:, n % 2, h, :],
                                                                last_h[:, n, h:h + 1], ALU.mult, ALU.add), f"s{h}_{n}")
                    if n + 1 in DVE_B:
                        c_pe_b.wait(dve, c, f"B{n + 1}")
                        c_db_dve.done(nc.vector.tensor_tensor(DB[:, (n + 1) % 2, :, :], DTX[:, rs, :, :],
                                                          PSB[:, :].unsqueeze(1).broadcast_to([P, HALVES, CH]),
                                                          ALU.mult), f"db{n + 1}")
                    c_dve.wait(dve, c, f"s1_{n}")
                    c_dve.done(nc.vector.tensor_copy(last_h[:, n, :].rearrange("p (h o) -> p h o", o=1),
                                                     HS[:, n % 2, :, CH - 1:CH]), f"last{n}")
                    c_pe_c.wait(dve, c, f"C{n}")
                    cb, nb = back(c, n, 2)
                    c_pe_y.wait(dve, cb, f"y{nb}")
                    c_dve.done(nc.vector.tensor_tensor(GS[:, n % 2, :, :], HS[:, n % 2, :, :],
                                                       PSC[:, :].unsqueeze(1).broadcast_to([P, HALVES, CH]),
                                                       ALU.mult), f"g{n}")
                if post:
                    if n == 0:
                        c_pe_y.wait(dve, co, f"y{NS - 1}")
                        for h in range(HALVES):
                            last = nc.vector.scalar_tensor_tensor(YV[:, h, :], XS[:, ro, h, :], cols[:, DPR, h:h + 1],
                                                                  PSY[:, h, :], ALU.mult, ALU.add)
                        o_dve.done(last, "y2")
                        o_dve.wait(dve, co, "y2")
                        o_dve.done(nc.vector.tensor_tensor(YV[:, :, :], YV[:, :, :], XS[:, ro, 2:4, :], ALU.mult), "y3")
                    if n == 1:
                        for b in range(2):
                            o_pe.wait(dve, co, f"out{b}")
                            o_dve.done(nc.vector.tensor_tensor(
                                RS[:, 2 * b:2 * b + 2, :], H0[:, ro, 2 * b:2 * b + 2, :],
                                PSW[bank(POST, f"out{b}")][:, :].rearrange("p (s n) -> p s n", s=2), ALU.add), f"res{b}")
                    if n == 2:
                        o_dve.wait(dve, co, "res1")
                        stats(o_dve, lambda s: RS[:, s, :], st_o, mv_o, co, ("stA", "agA"))
                    if n == 3:
                        o_act.wait(dve, co, "rsA")
                        o_dve.done(nc.vector.scalar_tensor_tensor(nm_o[:, :], mv_o[:, :, 0], -1.0, rs_o[:, :], ALU.mult,
                                                                  ALU.mult), "nmA")
                        dve.wait_ge(s_ag, (co + 1) * (16 * SUB))
                        dve.wait_ge(s_out, (c - 1) * (16 * SUB))
                        o_dve.done(nc.vector.tensor_scalar(rden[:, :, :], AG[:, :, D:AW], 1e-16, None, ALU.add), "den")
                        o_dve.wait(dve, co, "den")
                        o_dve.done(nc.vector.reciprocal(rden[:, :, :], rden[:, :, :]), "rden")
                        o_dve.wait(dve, co, "rden")
                        o_dve.done(nc.vector.tensor_tensor(
                            LV[:, :, :].rearrange("p s (h f) -> p s h f", h=NH),
                            AG[:, :, 0:D].rearrange("p s (h f) -> p s h f", h=NH),
                            rden[:, :, :].unsqueeze(3).broadcast_to([P, SUB, NH, FOUT]), ALU.mult), "loc")
                        o_dve.wait(dve, co, "loc")
                        o_pool.wait(dve, co, "hg")
                        o_dve.done(nc.vector.tensor_tensor(LV[:, :, :], LV[:, :, :], HG[:, :, :], ALU.add), "locs")
                        o_dve.wait(dve, co, "locs")
                        o_dve.done(nc.vector.tensor_scalar(LM[:, :, :], LV[:, :, :], 0.0, None, ALU.min), "mn")
                    if n == 4:
                        o_act.wait(dve, co, "elu")
                        o_dve.done(nc.vector.scalar_tensor_tensor(LV[:, :, :], LV[:, :, :], 0.0, LM[:, :, :], ALU.max,
                                                                  ALU.add), "elu")
                        o_dve.wait(dve, co, "elu")
                        stats(o_dve, lambda s: LV[:, s, :], st_o, mv_o, co, ("stL", "agL"))
                    if n == 5:
                        o_act.wait(dve, co, "rsL")
                        o_dve.done(nc.vector.scalar_tensor_tensor(nm_o[:, :], mv_o[:, :, 0], -1.0, rs_o[:, :], ALU.mult,
                                                                  ALU.mult), "nmL")
                    if n == 9:
                        o_act.wait(dve, co, "g1")
                        o_pool.wait(dve, co, "diff")
                        o_dve.done(nc.vector.scalar_tensor_tensor(GT[:, :, :], GT[:, :, :], 1.0, DIFF[:, :, :], ALU.add,
                                                                  ALU.mult), "gm")
                        o_dve.wait(dve, co, "gm")
                        o_dve.done(nc.vector.scalar_tensor_tensor(HAT[:, :, :], GT[:, :, :], 0.5, HAT[:, :, :], ALU.mult,
                                                                  ALU.add), "h")
                    if n in (13, 14):
                        b = n - 13
                        o_pe.wait(dve, co, f"ff2_{b}")
                        for s in range(2):
                            last = nc.vector.bn_stats(st_o[:, 2 * b + s, :],
                                                      PSW[bank(POST, f"ff2_{b}")][:, s * D:(s + 1) * D])
                        o_dve.done(last, f"st2{'ab'[b]}")
                    if n == 14:
                        o_dve.wait(dve, co, "st2b")
                        alone(dve)
                        for s in range(SUB):
                            last = nc.vector.bn_aggr(mv_o[:, s, :], st_o[:, s, :])
                        o_dve.done(last, "ag2")
                        o_act.wait(dve, co, "rs2")
                        o_dve.done(nc.vector.scalar_tensor_tensor(nm_o[:, :], mv_o[:, :, 0], -1.0, rs_o[:, :], ALU.mult,
                                                                  ALU.mult), "nm2")
                    if n == 15:
                        o_act.wait(dve, co, "nr2")
                        o_dve.done(nc.vector.tensor_tensor(OUT[:, :, :], OUT[:, :, :],
                                                           row_bc[:, LN2G, :].unsqueeze(1).broadcast_to([P, SUB, D]),
                                                           ALU.mult), "fg")
                        o_dve.wait(dve, co, "fg")
                        o_pool.wait(dve, co, "xb")
                        o_dve.done(nc.vector.tensor_tensor(OUT[:, :, :], OUT[:, :, :], XB[:, :, :], ALU.add), "fo")
                if pre:
                    if n == 2:
                        dve.wait_ge(s_x, (cp + 1) * (16 * SUB))
                        stats(r_dve, lambda s: X[:, rp, s, :], st_p, mv_p, cp, ("stats", "aggr"))
                    if n == 3:
                        r_act.wait(dve, cp, "rstd")
                        r_dve.done(nc.vector.scalar_tensor_tensor(nm_p[:, :], mv_p[:, :, 0], -1.0, rs_p[:, :], ALU.mult,
                                                                  ALU.mult), "nmr")
                        r_dve.wait(dve, c, "c3")
                        r_dve.done(nc.vector.tensor_copy(XCP[:, :, 0:TAPS - 1], XCP[:, :, CH:CH + TAPS - 1]), "carry")
                    if n == 6:
                        r_act.wait(dve, cp, "in1")
                        r_dve.wait(dve, c, "dt")
                        for h in range(HALVES):
                            last = nc.vector.tensor_scalar(AZ[:, h, :], XCP[:, h, TAPS - 1:], conv_w[:, h, TAPS - 1:TAPS],
                                                           cols[:, CVB, h:h + 1], ALU.mult, ALU.add)
                        r_dve.done(last, "c0")
                        for t in range(1, TAPS):
                            r_dve.wait(dve, cp, f"c{t - 1}")
                            k = TAPS - 1 - t
                            for h in range(HALVES):
                                last = nc.vector.scalar_tensor_tensor(AZ[:, h, :], XCP[:, h, k:k + CH],
                                                                      conv_w[:, h, k:k + 1], AZ[:, h, :], ALU.mult, ALU.add)
                            r_dve.done(last, f"c{t}")
                    if n == 9:
                        r_pe.wait(dve, cp, "dbc")
                        w = PSW[bank(PRE, "dbc")][0:2 * NS, :]
                        r_dve.done(nc.vector.tensor_copy(BC3[0:2 * NS, rp, :], w), "hi")
                        r_dve.wait(dve, cp, "hi")
                        r_act.wait(dve, cp, "dtr")
                        r_dve.done(nc.vector.tensor_tensor(R1[:, :], w, BC3[0:2 * NS, rp, :], ALU.subtract), "r1")
                        r_dve.wait(dve, cp, "r1")
                        r_dve.done(nc.vector.tensor_copy(MID[:, :], R1[:, :]), "mid")
                        r_dve.wait(dve, cp, "mid")
                        r_dve.done(nc.vector.tensor_copy(BC3[2 * NS:4 * NS, rp, :], MID[:, :]), "mids")
                        r_dve.done(nc.vector.tensor_tensor(BC3[4 * NS:6 * NS, rp, :], R1[:, :], MID[:, :], ALU.subtract),
                                   "lo")
                    if n == 11:
                        r_act.wait(dve, cp, "w")
                        r_dve.done(nc.vector.scalar_tensor_tensor(AZ[:, 2:4, :], AZ[:, 2:4, :], -1.0, EX[:, 0:2, :],
                                                                  ALU.add, ALU.subtract), "corr")
                    if n == 12:
                        r_act.wait(dve, cp, "L")
                        r_dve.wait(dve, cp, "corr")
                        r_dve.done(nc.vector.tensor_tensor(AZ[:, 2:4, :], AZ[:, 0:2, :], AZ[:, 2:4, :], ALU.subtract),
                                   "lsum")
                    if n == 13:
                        r_pool.wait(dve, cp, "series")
                        r_dve.wait(dve, cp, "lsum")
                        r_dve.done(nc.vector.tensor_scalar(EX[:, 0:2, :], EX[:, 0:2, :], SMALL, None, ALU.is_lt), "small")
                        r_dve.wait(dve, cp, "small")
                        alone(dve)
                        r_dve.done(nc.vector.copy_predicated(AZ[:, 2:4, :], EX[:, 0:2, :].bitcast(I32), DT[:, rp, :, :]),
                                   "pick")
                    if n == 14:
                        r_dve.wait(dve, cp, "pick")
                        r_dve.done(nc.vector.tensor_tensor(DT[:, rp, :, :], AZ[:, 2:4, :], EX[:, 2:4, :], ALU.add), "dt")
                        r_dve.wait(dve, cp, "dt")
                        r_dve.done(nc.vector.tensor_tensor(DTX[:, rp, :, :], DT[:, rp, :, :], XS[:, rp, 0:2, :], ALU.mult),
                                   "dtx")

            periods(dve, slot)


def kernel(**inputs):
    import numpy as np
    import concourse.bacc as bacc
    from concourse.bass_utils import run_bass_kernel_spmd as run

    w = {k[len("L0_gnn_"):]: np.asarray(v) for k, v in inputs.items() if k.startswith("L0_gnn_")}
    xp = w["x_proj_w"]
    xp = np.concatenate([xp[RANK:], xp[:RANK]], axis=0)
    arrays = {
        "x": inputs["x"], "src": inputs["src"], "dst": inputs["dst"], "noise": inputs["node_vec"],
        "gat_w": w["gat_w"], "gat_wT": w["gat_w"].T, "gat_a_src": w["gat_a_src"], "gat_a_tgt": w["gat_a_tgt"],
        "gat_b": w["gat_b"], "ln_local_g": w["ln_local_g"], "ln_local_b": w["ln_local_b"],
        "ln_global_g": w["ln_global_g"], "ln_global_b": w["ln_global_b"], "ln2_g": w["ln2_g"], "ln2_b": w["ln2_b"],
        "in_projT": w["in_proj_w"].T, "conv_w": w["conv_w"], "conv_b": w["conv_b"], "x_projT": xp.T,
        "dt_projT": w["dt_proj_w"].T, "dt_proj_b": w["dt_proj_b"], "A_log": w["A_log"], "D_param": w["D_param"],
        "out_projT": w["out_proj_w"].T, "wlT": w["wl"].T, "wgT": w["wg"].T, "ff1T": w["ff1_w"].T,
        "ff1_b": w["ff1_b"], "ff2T": w["ff2_w"].T, "ff2_b": w["ff2_b"],
    }
    arrays = {f"in_{k}": np.ascontiguousarray(v) for k, v in arrays.items()}
    nc = bacc.Bacc("TRN2", target_bir_lowering=False, num_devices=1)
    aps = {k[3:]: nc.dram_tensor(k, v.shape, mybir.dt.from_np(v.dtype), kind="ExternalInput").ap()
           for k, v in arrays.items()}
    out = nc.dram_tensor("out_x", arrays["in_x"].shape, F32, kind="ExternalOutput").ap()
    build(nc, aps, out)
    return run(nc, [arrays], core_ids=[0]).results[0]["out_x"]
```
